# Optimizing a Trainium2 kernel written in Bass

```python
import numpy as np
import jax
import jax.numpy as jnp

def _softmax(x, axis=-1):
    return jax.nn.softmax(x, axis=axis)

def _gelu(x):
    return jax.nn.gelu(x, approximate=True)

def _silu(x):
    return jax.nn.silu(x)

def _sigmoid(x):
    return jax.nn.sigmoid(x)

def _layernorm(x, axis=-1, eps=1e-05):
    m = jnp.mean(x, axis=axis, keepdims=True)
    v = jnp.var(x, axis=axis, keepdims=True)
    return (x - m) / jnp.sqrt(v + eps)

def _scatter_add(tgt, idx, src, axis=0):
    return tgt.at[idx].add(src)

def _segment_sum(src, seg, n):
    return jax.ops.segment_sum(src, seg, n)
kernel_name = 'mk_vit_tower_d2_tok_img256_r4_c4d653'

def setup_inputs(seed: int=0):
    np.random.seed(seed)
    _w = jnp.asarray

    def _rec_inputs():
        import jax
        import jax.numpy as jnp
        _rk = jax.random.key(seed)
        x = -7.10856e-05 + 0.999911 * jax.random.normal(jax.random.fold_in(_rk, 1), (128, 1, 64, 64), jnp.float32)
        return x
    x = _rec_inputs()

    def _L0_tok_setup():
        import jax, jax.numpy as jnp
        import numpy as np
        INV_SQRT2 = 0.7071067811865476

        def haar_dwt2(x):
            lo = (x[..., ::2] + x[..., 1::2]) * INV_SQRT2
            hi = (x[..., ::2] - x[..., 1::2]) * INV_SQRT2
            cA = (lo[..., ::2, :] + lo[..., 1::2, :]) * INV_SQRT2
            cH = (lo[..., ::2, :] - lo[..., 1::2, :]) * INV_SQRT2
            cV = (hi[..., ::2, :] + hi[..., 1::2, :]) * INV_SQRT2
            cD = (hi[..., ::2, :] - hi[..., 1::2, :]) * INV_SQRT2
            return (cA, (cH, cV, cD))

        def wavedec2_maps(x, levels):
            a = x
            details = []
            for _ in range(levels):
                a, d = haar_dwt2(a)
                details.append(d)
            maps = [a]
            for d in reversed(details):
                maps.extend(d)
            return maps
        key = jax.random.key(seed)
        k1, k2 = jax.random.split(key)
        B, H, W_img = (64, 256, 256)
        x = jax.random.normal(k1, (B, 1, H, W_img), dtype=jnp.float32)
        n_maps = 1 + 3 * 2
        W = jax.random.normal(k2, (n_maps, 64), dtype=jnp.float32) * (1.0 / np.sqrt(n_maps))
        b = jnp.zeros((64,), dtype=jnp.float32)
        return {'x': x, 'W': W, 'b': b}
    _L0_tok_all = _L0_tok_setup()
    _L0_tok_in = {k: v for k, v in _L0_tok_all.items() if k in ('W', 'b')}
    del _L0_tok_all

    def _L0_attn_setup():
        import jax, jax.numpy as jnp
        import numpy as np
        import math
        N, HW, D = (8, 4096, 64)
        HEADS = 8
        key = jax.random.key(seed)
        ks = jax.random.split(key, 9)
        s = 1.0 / math.sqrt(D)
        return {'x': jax.random.normal(ks[0], (N, HW, D), jnp.float32), 'Wk': jax.random.normal(ks[1], (D, D), jnp.float32) * s, 'bk': jax.random.normal(ks[2], (D,), jnp.float32) * 0.01, 'Wq': jax.random.normal(ks[3], (D, D), jnp.float32) * s, 'bq': jax.random.normal(ks[4], (D,), jnp.float32) * 0.01, 'Wv': jax.random.normal(ks[5], (D, D), jnp.float32) * s, 'bv': jax.random.normal(ks[6], (D,), jnp.float32) * 0.01, 'Wr': jax.random.normal(ks[7], (D, D), jnp.float32) * s, 'br': jax.random.normal(ks[8], (D,), jnp.float32) * 0.01}
    _L0_attn_all = _L0_attn_setup()
    _L0_attn_in = {k: v for k, v in _L0_attn_all.items() if k in ('Wk', 'bk', 'Wq', 'bq', 'Wv', 'bv', 'Wr', 'br')}
    del _L0_attn_all

    def _L0_ffn_setup():
        import jax, jax.numpy as jnp
        import numpy as np
        D_MODEL = 64
        N_EXPERTS = 16
        HIDDEN = 128
        SCALE = 0.02
        key = jax.random.key(seed)
        ks = jax.random.split(key, 5)
        x = jax.random.normal(ks[0], (4, 2048, D_MODEL), dtype=jnp.float32)
        gate_w = jax.random.normal(ks[1], (D_MODEL, N_EXPERTS), dtype=jnp.float32) * SCALE
        gate_b = jnp.zeros((N_EXPERTS,), dtype=jnp.float32)
        w1 = jax.random.normal(ks[2], (N_EXPERTS, D_MODEL, HIDDEN), dtype=jnp.float32) * SCALE
        w2 = jax.random.normal(ks[3], (N_EXPERTS, D_MODEL, HIDDEN), dtype=jnp.float32) * SCALE
        w3 = jax.random.normal(ks[4], (N_EXPERTS, HIDDEN, D_MODEL), dtype=jnp.float32) * SCALE
        return {'x': x, 'gate_w': gate_w, 'gate_b': gate_b, 'w1': w1, 'w2': w2, 'w3': w3}
    _L0_ffn_all = _L0_ffn_setup()
    _L0_ffn_in = {k: v for k, v in _L0_ffn_all.items() if k in ('gate_w', 'gate_b', 'w1', 'w2', 'w3')}
    del _L0_ffn_all

    def _L1_attn_setup():
        import jax, jax.numpy as jnp
        import numpy as np
        D_MODEL = 64
        N_HEAD = 8

        def _l1_scores(q, k):
            scale = 1.0 / np.sqrt(q.shape[-1]).astype(np.float32)
            q_sbhw = q.transpose(1, 0, 2, 3)

            def one_query(qs):
                return -jnp.sum(jnp.abs(qs[:, None, :, :] - k), axis=-1) * scale
            s = jax.lax.map(one_query, q_sbhw)
            return s.transpose(1, 0, 2, 3)
        key = jax.random.key(seed)
        ks = jax.random.split(key, 3)
        b, t = (4, 250)
        x = jax.random.normal(ks[0], (b, t, D_MODEL), jnp.float32)
        wqv_w = 0.005 * jax.random.normal(ks[1], (3 * N_HEAD * D_MODEL, D_MODEL), jnp.float32)
        wqv_b = jnp.zeros((3 * N_HEAD * D_MODEL,), jnp.float32)
        wk = 0.005 * jnp.ones((N_HEAD, D_MODEL), jnp.float32)
        fanin_w = 0.005 * jax.random.normal(ks[2], (D_MODEL, D_MODEL), jnp.float32)
        fanin_b = jnp.zeros((D_MODEL,), jnp.float32)
        return dict(x=x, wqv_w=wqv_w, wqv_b=wqv_b, wk=wk, fanin_w=fanin_w, fanin_b=fanin_b)
    _L1_attn_all = _L1_attn_setup()
    _L1_attn_in = {k: v for k, v in _L1_attn_all.items() if k in ('wqv_w', 'wqv_b', 'wk', 'fanin_w', 'fanin_b')}
    del _L1_attn_all

    def _L1_ffn_setup():
        import jax, jax.numpy as jnp
        import numpy as np
        B, T, IN_DIM = (64, 64, 64)
        HID, OUT_DIM = (128, 64)
        N_LAYERS, N_EXPERTS, N_SHARED = (2, 16, 1)
        key = jax.random.key(seed)
        ks = jax.random.split(key, 10)
        s = 0.02
        x = jax.random.normal(ks[0], (B, T, IN_DIM), dtype=jnp.float32)
        route_id = jax.random.randint(ks[1], (B,), 0, N_EXPERTS)
        Wi = jax.random.normal(ks[2], (HID, IN_DIM), dtype=jnp.float32) * s
        bi = jnp.zeros((HID,), dtype=jnp.float32)
        Wr = jax.random.normal(ks[3], (N_LAYERS, N_EXPERTS, HID, HID), dtype=jnp.float32) * s
        br = jax.random.normal(ks[4], (N_LAYERS, N_EXPERTS, HID), dtype=jnp.float32) * s
        Ws = jax.random.normal(ks[5], (N_LAYERS, N_SHARED, HID, HID), dtype=jnp.float32) * s
        bs = jax.random.normal(ks[6], (N_LAYERS, N_SHARED, HID), dtype=jnp.float32) * s
        Wo = jax.random.normal(ks[7], (OUT_DIM, HID), dtype=jnp.float32) * s
        bo = jnp.zeros((OUT_DIM,), dtype=jnp.float32)
        return {'x': x, 'route_id': route_id, 'Wi': Wi, 'bi': bi, 'Wr': Wr, 'br': br, 'Ws': Ws, 'bs': bs, 'Wo': Wo, 'bo': bo}
    _L1_ffn_all = _L1_ffn_setup()
    _L1_ffn_in = {k: v for k, v in _L1_ffn_all.items() if k in ('route_id', 'Wi', 'bi', 'Wr', 'br', 'Ws', 'bs', 'Wo', 'bo')}
    del _L1_ffn_all
    return {'x': x, 'L0_tok_W': _L0_tok_in['W'], 'L0_tok_b': _L0_tok_in['b'], 'L0_attn_Wk': _L0_attn_in['Wk'], 'L0_attn_bk': _L0_attn_in['bk'], 'L0_attn_Wq': _L0_attn_in['Wq'], 'L0_attn_bq': _L0_attn_in['bq'], 'L0_attn_Wv': _L0_attn_in['Wv'], 'L0_attn_bv': _L0_attn_in['bv'], 'L0_attn_Wr': _L0_attn_in['Wr'], 'L0_attn_br': _L0_attn_in['br'], 'L0_ffn_gate_w': _L0_ffn_in['gate_w'], 'L0_ffn_gate_b': _L0_ffn_in['gate_b'], 'L0_ffn_w1': _L0_ffn_in['w1'], 'L0_ffn_w2': _L0_ffn_in['w2'], 'L0_ffn_w3': _L0_ffn_in['w3'], 'L1_attn_wqv_w': _L1_attn_in['wqv_w'], 'L1_attn_wqv_b': _L1_attn_in['wqv_b'], 'L1_attn_wk': _L1_attn_in['wk'], 'L1_attn_fanin_w': _L1_attn_in['fanin_w'], 'L1_attn_fanin_b': _L1_attn_in['fanin_b'], 'L1_ffn_route_id': _L1_ffn_in['route_id'], 'L1_ffn_Wi': _L1_ffn_in['Wi'], 'L1_ffn_bi': _L1_ffn_in['bi'], 'L1_ffn_Wr': _L1_ffn_in['Wr'], 'L1_ffn_br': _L1_ffn_in['br'], 'L1_ffn_Ws': _L1_ffn_in['Ws'], 'L1_ffn_bs': _L1_ffn_in['bs'], 'L1_ffn_Wo': _L1_ffn_in['Wo'], 'L1_ffn_bo': _L1_ffn_in['bo']}

def reference(x, L0_tok_W, L0_tok_b, L0_attn_Wk, L0_attn_bk, L0_attn_Wq, L0_attn_bq, L0_attn_Wv, L0_attn_bv, L0_attn_Wr, L0_attn_br, L0_ffn_gate_w, L0_ffn_gate_b, L0_ffn_w1, L0_ffn_w2, L0_ffn_w3, L1_attn_wqv_w, L1_attn_wqv_b, L1_attn_wk, L1_attn_fanin_w, L1_attn_fanin_b, L1_ffn_route_id, L1_ffn_Wi, L1_ffn_bi, L1_ffn_Wr, L1_ffn_br, L1_ffn_Ws, L1_ffn_bs, L1_ffn_Wo, L1_ffn_bo):
    import jax
    import jax.numpy as jnp

    def _L0_tok_ref(x, W, b):
        import jax, jax.numpy as jnp
        import numpy as np
        INV_SQRT2 = 0.7071067811865476

        def haar_dwt2(x):
            lo = (x[..., ::2] + x[..., 1::2]) * INV_SQRT2
            hi = (x[..., ::2] - x[..., 1::2]) * INV_SQRT2
            cA = (lo[..., ::2, :] + lo[..., 1::2, :]) * INV_SQRT2
            cH = (lo[..., ::2, :] - lo[..., 1::2, :]) * INV_SQRT2
            cV = (hi[..., ::2, :] + hi[..., 1::2, :]) * INV_SQRT2
            cD = (hi[..., ::2, :] - hi[..., 1::2, :]) * INV_SQRT2
            return (cA, (cH, cV, cD))

        def wavedec2_maps(x, levels):
            a = x
            details = []
            for _ in range(levels):
                a, d = haar_dwt2(a)
                details.append(d)
            maps = [a]
            for d in reversed(details):
                maps.extend(d)
            return maps
        imgs = x[:, 0]
        B = imgs.shape[0]
        maps = wavedec2_maps(imgs, 2)
        proc = [jax.image.resize(m, (B, 8, 8), method='bilinear') for m in maps]
        feat = jnp.stack(proc, axis=1)
        feat = feat.reshape(B, feat.shape[1], 64).transpose(0, 2, 1)
        return feat @ W + b

    def _L0_attn_ref(x, Wk, bk, Wq, bq, Wv, bv, Wr, br):
        import jax, jax.numpy as jnp
        import numpy as np
        import math
        N, HW, D = (8, 4096, 64)
        HEADS = 8
        n, hw, d = x.shape
        heads = HEADS
        hk = d // heads
        hv = d // heads
        flat = x.reshape(n, d, hw)
        keys = jnp.einsum('kd,ndl->nkl', Wk, flat) + bk[None, :, None]
        queries = jnp.einsum('kd,ndl->nkl', Wq, flat) + bq[None, :, None]
        values = jnp.einsum('vd,ndl->nvl', Wv, flat) + bv[None, :, None]
        K = jax.nn.softmax(keys.reshape(n, heads, hk, hw), axis=3)
        Q = jax.nn.softmax(queries.reshape(n, heads, hk, hw), axis=2)
        V = values.reshape(n, heads, hv, hw)
        context = jnp.einsum('nhkl,nhvl->nhkv', K, V)
        att = jnp.einsum('nhkv,nhkl->nhvl', context, Q)
        agg = att.reshape(n, heads * hv, hw)
        out = jnp.einsum('dv,nvl->ndl', Wr, agg) + br[None, :, None]
        return out.reshape(n, hw, d)

    def _L0_ffn_ref(x, gate_w, gate_b, w1, w2, w3):
        import jax, jax.numpy as jnp
        import numpy as np
        D_MODEL = 64
        N_EXPERTS = 16
        HIDDEN = 128
        SCALE = 0.02
        n_experts = w1.shape[0]
        logits = jnp.einsum('bsd,de->bse', x, gate_w) + gate_b
        probs = jax.nn.softmax(logits, axis=-1)
        top_probs, top_idx = jax.lax.top_k(probs, 2)
        top_probs = top_probs / jnp.sum(top_probs, axis=-1, keepdims=True)
        dispatch = jnp.sum(jax.nn.one_hot(top_idx, n_experts, dtype=x.dtype) * top_probs[..., None], axis=-2)
        h1 = jnp.einsum('bsd,edh->bseh', x, w1)
        h2 = jnp.einsum('bsd,edh->bseh', x, w2)
        hidden = jax.nn.silu(h1) * h2
        expert_out = jnp.einsum('bseh,eho->bseo', hidden, w3)
        return jnp.einsum('bseo,bse->bso', expert_out, dispatch)

    def _L1_attn_ref(x, wqv_w, wqv_b, wk, fanin_w, fanin_b):
        import jax, jax.numpy as jnp
        import numpy as np
        D_MODEL = 64
        N_HEAD = 8

        def _l1_scores(q, k):
            scale = 1.0 / np.sqrt(q.shape[-1]).astype(np.float32)
            q_sbhw = q.transpose(1, 0, 2, 3)

            def one_query(qs):
                return -jnp.sum(jnp.abs(qs[:, None, :, :] - k), axis=-1) * scale
            s = jax.lax.map(one_query, q_sbhw)
            return s.transpose(1, 0, 2, 3)
        b, t, d = x.shape
        h = N_HEAD
        v = (x @ wqv_w.T + wqv_b).reshape(b, t, 3 * h, d)
        q, vf, vb = (v[:, :, :h], v[:, :, h:2 * h], v[:, :, 2 * h:])
        k = x[:, :, None, :] * wk[None, None]
        a = _l1_scores(q, k)
        a = jnp.concatenate([a, jnp.zeros((b, 1, t, h), a.dtype)], axis=1)
        a = jax.nn.softmax(a, axis=1)[:, :t]
        bf = jnp.einsum('bsdh,bshw->bdhw', a, vf)
        bb = jnp.einsum('bdsh,bshw->bdhw', a, vb)
        o = (bf + bb).sum(axis=2).reshape(b, t, d)
        y = o * jax.nn.sigmoid(1.702 * o)
        y = y @ fanin_w.T + fanin_b
        return x + y

    def _L1_ffn_ref(x, route_id, Wi, bi, Wr, br, Ws, bs, Wo, bo):
        import jax, jax.numpy as jnp
        import numpy as np
        B, T, IN_DIM = (64, 64, 64)
        HID, OUT_DIM = (128, 64)
        N_LAYERS, N_EXPERTS, N_SHARED = (2, 16, 1)
        flat = x.reshape(-1, x.shape[-1])
        n_tok = flat.shape[0]
        route = jnp.repeat(route_id, n_tok // route_id.shape[0])
        h = jax.nn.relu(flat @ Wi.T + bi)
        n_layers, n_experts = (Wr.shape[0], Wr.shape[1])
        for l in range(n_layers):
            shared = (jnp.einsum('nd,shd->snh', h, Ws[l]) + bs[l][:, None, :]).mean(axis=0)
            routed = jnp.zeros_like(h)
            for e in range(n_experts):
                ye = h @ Wr[l, e].T + br[l, e]
                routed = routed + jnp.where((route == e)[:, None], ye, 0.0)
            h = jax.nn.relu(shared + routed + h)
        out = h @ Wo.T + bo
        return out.reshape(*x.shape[:-1], out.shape[-1])
    h = _L0_tok_ref(x, L0_tok_W, L0_tok_b)
    h = h + _L0_attn_ref(_layernorm(h, axis=-1), L0_attn_Wk, L0_attn_bk, L0_attn_Wq, L0_attn_bq, L0_attn_Wv, L0_attn_bv, L0_attn_Wr, L0_attn_br)
    h = h + _L0_ffn_ref(_layernorm(h, axis=-1), L0_ffn_gate_w, L0_ffn_gate_b, L0_ffn_w1, L0_ffn_w2, L0_ffn_w3)
    h = h + _L1_attn_ref(_layernorm(h, axis=-1), L1_attn_wqv_w, L1_attn_wqv_b, L1_attn_wk, L1_attn_fanin_w, L1_attn_fanin_b)
    h = h + _L1_ffn_ref(_layernorm(h, axis=-1), L1_ffn_route_id, L1_ffn_Wi, L1_ffn_bi, L1_ffn_Wr, L1_ffn_br, L1_ffn_Ws, L1_ffn_bs, L1_ffn_Wo, L1_ffn_bo)
    return h

_drawn_inputs = setup_inputs


def setup_inputs(seed=0):
    import zlib

    import numpy as np

    out = dict(_drawn_inputs(seed))
    spreads = {'L0_tok_b': (0.0, 0.1),
     'L0_ffn_gate_b': (0.0, 0.8),
     'L1_attn_wqv_b': (0.0, 2.0),
     'L1_attn_wk': (0.004999999888241291, 0.6),
     'L1_attn_fanin_b': (0.0, 0.1),
     'L1_ffn_bi': (0.0, 0.762),
     'L1_ffn_bo': (0.0, 0.1)}
    factors = {'L0_attn_bk': 200.0,
     'L0_attn_bq': 8.0,
     'L0_attn_bv': 5.956,
     'L0_attn_br': 7.891,
     'L0_ffn_gate_w': 8.0,
     'L0_ffn_w1': 8.0,
     'L0_ffn_w2': 8.0,
     'L0_ffn_w3': 8.0,
     'L1_attn_wqv_w': 200.0,
     'L1_attn_fanin_w': 64.0,
     'L1_ffn_Wi': 3.549,
     'L1_ffn_Wr': 8.0,
     'L1_ffn_br': 8.0,
     'L1_ffn_Ws': 8.0,
     'L1_ffn_bs': 8.0}
    for name, (base, spread) in spreads.items():
        noise = np.random.default_rng([zlib.crc32(name.encode()), seed]).standard_normal(out[name].shape)
        drawn = base * np.exp(spread * noise) if base else spread * noise
        out[name] = jnp.asarray(drawn.astype(out[name].dtype))
    for name, factor in factors.items():
        out[name] = (out[name] * factor).astype(out[name].dtype)
    return out
```

```python
from contextlib import ExitStack

import numpy as np

import concourse.bass as bass
from concourse import mybir

F32 = mybir.dt.float32
F16 = mybir.dt.float16
I32 = mybir.dt.int32
ALU = mybir.AluOpType
ACT = mybir.ActivationFunctionType
AX = mybir.AxisListType

P = 128
IMGS = 128
S = 64
D = 64
PAIRS = IMGS // 2
HEADS = 8
EXPERTS = 16
HID = 128
EPS = 1e-5

G4 = PAIRS // 4
G8 = PAIRS // 8
POOLED = (1, 4, 7, 10, 17, 20, 23, 26)
REDUCED = tuple(k for k in range(32) if k not in POOLED)
W_SCALE = 64.0
LO_SCALE = 2048.0
KA = 96
QK = HEADS * D


def haar_rows(n):
    lo, hi = np.zeros((n // 2, n)), np.zeros((n // 2, n))
    for k in range(n // 2):
        lo[k, 2 * k] = lo[k, 2 * k + 1] = hi[k, 2 * k] = np.sqrt(0.5)
        hi[k, 2 * k + 1] = -np.sqrt(0.5)
    return lo, hi


def resize_rows(n, to=8):
    scale = n / to
    centre = (np.arange(to) + 0.5) * scale - 0.5
    w = np.maximum(0.0, 1.0 - np.abs(centre[:, None] - np.arange(n)[None, :]) / scale)
    return w / w.sum(1, keepdims=True)


def wavelet_operators():
    l1, h1 = haar_rows(64)
    l2, h2 = haar_rows(32)
    return np.stack([resize_rows(16) @ l2 @ l1, resize_rows(16) @ h2 @ l1, resize_rows(32) @ l1, resize_rows(32) @ h1])


MAPS = [(0, 0), (1, 0), (0, 1), (1, 1), (3, 2), (2, 3), (3, 3)]


def constants():
    ops = wavelet_operators()
    rows = np.zeros((2, 64, 4, 2, 8))
    for b in range(2):
        rows[b, :, :, b, :] = ops.transpose(2, 0, 1)
    cols = np.zeros((7, 2, 8, 2, 64))
    for m, (row, col) in enumerate(MAPS):
        cols[m, row % 2, :, row // 2] = ops[col]
    pick = np.zeros((4, 32, 8, 4, 32))
    for g in range(8):
        for x in range(4):
            for y in range(32):
                pick[0, 8 * x + g, g, x, y] = 1.0
                pick[1, 8 * x + g, g, x, y] = 1.0 / LO_SCALE
                pick[2, y, g, x, y] = -1.0
                pick[3, y, g, x, y] = -1.0 / LO_SCALE
    same_head = np.kron(np.eye(16), np.ones((8, 8)))
    rank = np.broadcast_to(EXPERTS - np.arange(EXPERTS), (P, EXPERTS))
    return {
        "c_rows": rows.reshape(P, 64).astype(np.float32),
        "c_cols": cols.reshape(7, 2 * 8 * P).astype(np.float32),
        "c_pick": pick.reshape(P, 8 * P).astype(np.float16),
        "c_head": same_head.astype(np.float32),
        "c_ident": np.eye(P, dtype=np.float32),
        "c_rank": np.ascontiguousarray(rank).astype(np.float32),
    }


def build(nc, a, out, scratch):
    with ExitStack() as ctx:
        def sb(name, shape, dt=F32):
            return ctx.enter_context(nc.sbuf_tensor(name, shape, dt))

        def sem(name):
            return ctx.enter_context(nc.semaphore(name))

        h = sb("h", [P, PAIRS, D])
        xn = sb("xn", [P, PAIRS + 4, D])
        big = sb("big", [P, PAIRS * D])
        big2 = sb("big2", [P, 2 * EXPERTS * (HID + 1)])
        ident = sb("ident", [P, P])
        stat = sb("stat", [P, 6, PAIRS])

        c_rows = sb("c_rows_sb", [P, 64])
        c_cols = sb("c_cols_sb", [7, 2, 8, P])
        tok_w = sb("tok_w", [7, D])
        tok_b = sb("tok_b", [P, D])
        big3 = sb("big3", [P, 3088])
        mapw = big3[:, 0:1024].rearrange("p (o n) -> p o n", o=2)
        rowed = big3[:, 1024:3072].rearrange("p (o q r) -> p o q r", o=2, q=PAIRS)
        wk_bd = sb("wk_bd", [P, P])
        wqv_bd = sb("wqv_bd", [P, 2, P])
        wr_bd = sb("wr_bd", [P, P])
        bk2 = sb("bk2", [P, 1])
        br2 = sb("br2", [P, 1])
        bqv = sb("bqv", [P, 2, 2, D])
        same_head = sb("same_head", [P, P])
        xs8 = sb("xs8", [P, 8 * D])
        kexp = sb("kexp", [P, 8, D])
        kst = sb("kst", [P, 3, 8])
        qv = sb("qv", [P, 4, 2, P])
        qst = sb("qst", [P, 3, 4, 16])
        kT = sb("kT", [P, 2, 4, P])
        qT = sb("qT", [P, 512])
        ctx_bd = sb("ctx_bd", [P, 8, P])
        att_sb = sb("att_sb", [P, 512])

        w12_hi = sb("w12_hi", [P, 2, EXPERTS, HID], F16)
        w12_lo = sb("w12_lo", [P, 2, EXPERTS, HID], F16)
        w3 = sb("w3", [HID, EXPERTS, D])
        gate = sb("gate", [KA, EXPERTS])
        rank = sb("rank", [P, EXPERTS])
        xs4 = sb("xs4", [P, 4 * D])
        xT4 = sb("xT4", [KA, 512])
        x2 = sb("x2", [P, 2, 512], F16)
        logit = sb("logit", [P, 4, EXPERTS])
        gsc = sb("gsc", [P, 3, 4, EXPERTS])
        gst = sb("gst", [P, 7, 4])
        disp = sb("disp", [P, 2, 4, EXPERTS])
        silu = sb("silu", [P, 2, 512])
        hid = sb("hid", [P, 2, 512])
        yw = sb("yw", [P, 2, 2, 4 * D])
        acc = sb("acc", [P, 4 * D])
        wqv = sb("wqv", [KA, 3 * QK])
        fan = sb("fan", [KA, D])
        wk_b = sb("wk_b", [P, HEADS, D])
        pick = sb("pick", [P, 8, P], F16)
        xs1 = sb("xs1", [P, 2 * D])
        xT1 = sb("xT1", [KA, 2, P])
        xTq = sb("xTq", [KA, P])
        kf = sb("kf", [P, HEADS, D])
        lo_f = sb("lo_f", [P, 2, QK])
        qk = sb("qk", [P, 2, 2, QK], F16)
        blocks = sb("blocks", [P, 2, 2, 2, QK], F16)
        score = sb("score", [P, 2, 2, 2, 8, HEADS])
        expd = sb("expd", [P, 2, 256])
        attn = sb("attn", [P, S, HEADS])
        zst = sb("zst", [P, 3, HEADS])
        attk = sb("attk", [P, HEADS, S])
        attq = sb("attq", [P, 4, P])
        vf = sb("vf", [P, 2, 2, 4, D])
        vb = sb("vb", [P, 2, HEADS, D])
        osb = sb("osb", [P, 4, D])
        yT = sb("yT", [KA, P])
        hx = sb("hx", [P, D])
        wi = sb("wi", [KA, HID])
        wc = big2[:, 0:2 * EXPERTS * (HID + 1)].rearrange("p (l e n) -> p l e n", l=2, e=EXPERTS)
        ws = sb("ws", [HID, 2, HID + 1])
        wo = sb("wo", [HID, D])
        bo = sb("bo", [P, D])
        route = sb("route", [1, PAIRS], I32)
        xs5 = sb("xs5", [P, 2, 4 * D])
        xT5 = big3[0:KA, 2064:3088].rearrange("p (a n) -> p a n", a=2)
        wsel = big3[:, 0:2064].rearrange("p (l a j n) -> p l a j n", l=2, a=2, j=4)
        hm = big[:, 0:3072].rearrange("p (l a n) -> p l a n", l=3, a=2)
        hb = big[:, 3072:3584].rearrange("p (a n) -> p a n", a=2)
        fin = big[:, 3584:4096].rearrange("p (a n) -> p a n", a=2)

        pp = ctx.enter_context(nc.psum_tensor("pp", [P, 8, 512], F32))
        ps = [pp[:, i, :] for i in range(8)]

        x_in = [sem(f"x_in{k}") for k in range(4)]
        tok_in = sem("tok_in")
        attn_in = sem("attn_in")
        zeroed = sem("zeroed")
        mapw_ps = sem("mapw_ps")
        mapw_sb = sem("mapw_sb")
        rowed_ps = sem("rowed_ps")
        rowed_sb = sem("rowed_sb")
        tok_ps = sem("tok_ps")
        tok_sb = sem("tok_sb")
        tok_out = sem("tok_out")
        h_in = sem("h_in")
        ln_step = [sem(f"ln_step{k}") for k in range(4)]
        ln_sd = [sem(f"ln_sd{k}") for k in range(4)]
        xn_ready = [sem(f"xn_ready{k}") for k in range(4)]
        h_ready = [sem(f"h_ready{k}") for k in range(4)]

        x_all = big2[:, 0:PAIRS * D].rearrange("p (n j) -> p n j", j=64)
        tok_rows = big[:].rearrange("p (u n) -> p u n", u=8)

        absd = big[:, 0:2048].rearrange("p (a n w) -> p a n w", a=2, w=D)

        B = {n: sem("b_" + n) for n in (
            "xs", "xs_free", "k_ps", "k_sb", "kmax", "kcen", "kexp", "ksum", "krec", "qv_ps", "qv_sb", "qmax", "qcen",
            "qexp", "qsum", "qrec", "qnorm", "kT_ps", "kT_sb", "qT_ps", "qT_sb", "ctx_ps", "ctx_sb", "att_ps", "att_sb",
            "out_ps", "out_sb")}

        moe_in = sem("moe_in")
        w12_in = sem("w12_in")
        w12_ready = sem("w12_ready")
        pads = sem("pads")
        C = {n: sem("c_" + n) for n in (
            "xs", "xT_ps", "xT_sb", "xh", "xl", "logit_ps", "logit_sb", "gate", "gap", "tanh", "disp",
            "h1_ps", "h2_ps", "silu", "hid", "y_ps", "yw", "acc", "sum")}
        l1_in = sem("l1_in")
        X = {n: sem("d_" + n) for n in (
            "xs", "xT_ps", "xT_sb", "xTq", "q_ps", "qh", "qd", "ql", "kf", "kh", "kd", "kl", "tb0", "tb1",
            "diff", "red", "abs", "tree", "pooled", "exp", "attn", "z", "z1", "zr", "attk", "attq_ps", "attq", "o_ps", "sig", "den", "rden", "y",
            "yT_ps", "yT", "fan_ps", "hx", "sum", "vb_ps", "vb", "vf_ps", "vf")}
        mlp_in = sem("mlp_in")
        wc_ready = sem("wc_ready")
        M = {n: sem("e_" + n) for n in (
            "xs", "xT_ps", "xT", "h0_ps", "h0", "sel0", "sel1", "h1_ps", "h1", "h2_ps", "h2", "o_ps", "hb", "fin", "out", "free", "sent")}

        block = ctx.enter_context(nc.Block())

        def layernorm_dve(dve, k):
            step = ln_step[k]
            total, mean, var, sd, r, t = (stat[:, n, :] for n in range(6))
            x = xn[:, 0:PAIRS, :]
            sq = big[:].rearrange("p (n d) -> p n d", d=D)
            dve.tensor_reduce(total, h[:], AX.X, ALU.add).then_inc(step, 1)
            dve.wait_ge(step, 1)
            dve.tensor_scalar(mean, total, 1.0 / D, None, ALU.mult).then_inc(step, 1)
            dve.wait_ge(step, 2)
            dve.tensor_tensor(x, h[:], mean.unsqueeze(2).to_broadcast([P, PAIRS, D]), ALU.subtract).then_inc(step, 1)
            dve.wait_ge(step, 3)
            dve.tensor_tensor(sq, x, x, ALU.mult).then_inc(step, 1)
            dve.wait_ge(step, 4)
            dve.tensor_reduce(total, sq, AX.X, ALU.add).then_inc(step, 1)
            dve.wait_ge(step, 5)
            dve.tensor_scalar(var, total, 1.0 / D, EPS, ALU.mult, ALU.add).then_inc(step, 1)
            dve.wait_ge(ln_sd[k], 1)
            dve.reciprocal(r, sd).then_inc(step, 1)
            dve.wait_ge(step, 7)
            dve.tensor_tensor(t, r, r, ALU.mult).then_inc(step, 1)
            dve.wait_ge(step, 8)
            dve.tensor_tensor(t, t, var, ALU.mult).then_inc(step, 1)
            dve.wait_ge(step, 9)
            dve.tensor_scalar(t, t, -0.5, 1.5, ALU.mult, ALU.add).then_inc(step, 1)
            dve.wait_ge(step, 10)
            dve.tensor_tensor(r, r, t, ALU.mult).then_inc(step, 1)
            dve.wait_ge(step, 11)
            dve.tensor_tensor(x, x, r.unsqueeze(2).to_broadcast([P, PAIRS, D]), ALU.mult).then_inc(xn_ready[k], 1)

        def layernorm_act(act, k):
            act.wait_ge(ln_step[k], 6)
            nc.scalar.activation(stat[:, 3, :], stat[:, 2, :], ACT.Sqrt).then_inc(ln_sd[k], 1)

        ATTN_IN = 16 * 18
        MOE_IN = 16 * 5
        L1_IN = 16 * 6
        MLP_IN = 16 * 6
        PADS = 14

        def ACC(_, g, k):
            return 15 * g + 2 * k + 1 if k >= 0 else 15 * (g - 1) + 2 * (k + 8) + 1

        w12_f = big2[:, 0:PAIRS * D].rearrange("p (w e n) -> p w e n", w=2, e=EXPERTS)

        @block.sync
        def _(sp):
            for k in range(4):
                sp.dma_start(x_all[:, 16 * k:16 * k + 16, :], a["x_rows"][:, 16 * k:16 * k + 16, :]).then_inc(x_in[k], 16)
            sp.dma_start(ident[:], a["c_ident"]).then_inc(attn_in, 16)
            sp.dma_start(same_head[:], a["c_head"]).then_inc(attn_in, 16)
            sp.wait_ge(zeroed, 1)
            for b in range(2):
                at = slice(64 * b, 64 * b + 64)
                sp.dma_start(wk_bd[at, at], a["wk0_t"]).then_inc(attn_in, 16)
                sp.dma_start(wqv_bd[at, 0, at], a["wq0_t"]).then_inc(attn_in, 16)
                sp.dma_start(wqv_bd[at, 1, at], a["wv0_t"]).then_inc(attn_in, 16)
                sp.dma_start(wr_bd[at, at], a["wr0_t"]).then_inc(attn_in, 16)
                sp.dma_start(bk2[at, :], a["L0_attn_bk"].unsqueeze(1)).then_inc(attn_in, 16)
                sp.dma_start(br2[at, :], a["L0_attn_br"].unsqueeze(1)).then_inc(attn_in, 16)
                sp.dma_start(bqv[:, 0, b, :], a["L0_attn_bq"].partition_broadcast(P)).then_inc(attn_in, 16)
                sp.dma_start(bqv[:, 1, b, :], a["L0_attn_bv"].partition_broadcast(P)).then_inc(attn_in, 16)
            rows = scratch.rearrange("(u m c) d -> u m (c d)", u=8, m=P)
            for u in range(8):
                sp.wait_ge(tok_sb, u + 1)
                sp.dma_start(rows[u], tok_rows[:, u, :]).then_inc(tok_out, 16)
            sp.wait_ge(tok_out, 16 * 8)
            sp.dma_start(h[:], scratch.rearrange("(n m) d -> m n d", m=P)).then_inc(h_in, 16)
            sp.wait_ge(rowed_ps, 4)
            for n, w in enumerate(("L0_ffn_w1", "L0_ffn_w2")):
                for b in range(2):
                    sp.dma_start(w12_f[64 * b:64 * b + 64, n, :, :], a[w].rearrange("e d n -> d e n")).then_inc(w12_in, 16)
            sp.wait_ge(pads, PADS)
            sp.dma_start(w3[:], a["L0_ffn_w3"].rearrange("e n o -> n e o")).then_inc(moe_in, 16)
            sp.dma_start(gate[0:D, :], a["L0_ffn_gate_w"]).then_inc(moe_in, 16)
            sp.dma_start(gate[D:D + 1, :], a["L0_ffn_gate_b"].unsqueeze(0)).then_inc(moe_in, 16)
            sp.dma_start(rank[:], a["c_rank"]).then_inc(moe_in, 16)
            sp.dma_start(pick[:].rearrange("p a b -> p (a b)"), a["c_pick"]).then_inc(moe_in, 16)
            sp.dma_start(wqv[0:D, :], a["wqv_t"]).then_inc(l1_in, 16)
            sp.dma_start(wqv[D:D + 1, :], a["L1_attn_wqv_b"].unsqueeze(0)).then_inc(l1_in, 16)
            sp.dma_start(wk_b[:], a["L1_attn_wk"].partition_broadcast(P)).then_inc(l1_in, 16)
            sp.dma_start(fan[0:D, :], a["fanin_t"]).then_inc(l1_in, 16)
            sp.dma_start(fan[D:D + 1, :], a["L1_attn_fanin_b"].unsqueeze(0)).then_inc(l1_in, 16)
            sp.dma_start(route[:], a["L1_ffn_route_id"].unsqueeze(0)).then_inc(l1_in, 16)
            sp.dma_start(wi[0:D, :], a["wi_t"]).then_inc(mlp_in, 16)
            sp.dma_start(wi[D:D + 1, :], a["L1_ffn_bi"].unsqueeze(0)).then_inc(mlp_in, 16)
            sp.wait_ge(w12_ready, 2)
            sp.dma_start(wc, a["wrb_t"]).then_inc(mlp_in, 16)
            sp.dma_start(ws[:], a["wsb_t"]).then_inc(mlp_in, 16)
            sp.dma_start(wo[:], a["wo_t"]).then_inc(mlp_in, 16)
            sp.dma_start(bo[:], a["L1_ffn_bo"].partition_broadcast(P)).then_inc(mlp_in, 16)

            def fill_blocks(made, b):
                for kind in range(2):
                    for part in range(2):
                        ready = (("qh", 1), ("ql", 1), ("kh", 1), ("kl", 1))[2 * kind + part]
                        if b == 0:
                            sp.wait_ge(X[ready[0]], made)
                        for half in range(2):
                            src = qk[64 * b + 32 * half:64 * b + 32 * half + 32, kind, part, :]
                            to = slice(64 * kind + 32 * part, 64 * kind + 32 * part + 32)
                            dst = blocks[to, b, :, half, :] if kind == 0 else blocks[to, b, half, :, :]
                            sp.dma_start(dst, src.unsqueeze(1).to_broadcast([32, 2, QK])).then_inc(X[f"tb{b}"], 16)

            def spread(p, b):
                sp.wait_ge(X["exp"], 2 * p + b + 1)
                for j in range(2):
                    for x in range(4):
                        sp.dma_start(attn[64 * b + 32 * j:64 * b + 32 * j + 32, 16 * x:16 * x + 16, :].rearrange("p s h -> p (s h)"),
                                     expd[32 * x:32 * x + 32, b, P * j:P * j + P]).then_inc(X["attn"], 16)

            def pair(made, first):
                p = made - 2
                if not first:
                    sp.wait_ge(X["diff"], 32 * p)
                    fill_blocks(None, 1)
                sp.wait_ge(X["diff"], 32 * p + 16)
                fill_blocks(made, 0)
                spread(p, 0)
                spread(p, 1)

            fill_blocks(1, 0)
            fill_blocks(1, 1)
            pair(2, True)
            with sp.Fori(3, PAIRS + 2) as made:
                pair(made, False)
            sp.wait_ge(X["attn"], 16 * 16 * PAIRS)
            sp.wait_ge(X["tb0"], 16 * 8 * (PAIRS + 1))
            sp.sem_inc(M["sent"], 1)
            with sp.Fori(0, G4 // 2) as i:
                for b in range(2):
                    sp.wait_ge(M["fin"], 2 * i + b + 1)
                    sp.dma_start(out.rearrange("(p b) s d -> (b s) p d", b=2)[:, bass.ds(8 * i + 4 * b, 4), :],
                                 fin[:, b, :].rearrange("p (n d) -> p n d", d=D)).then_inc(M["out"], 16)
                sp.wait_ge(M["out"], 32 * i + 32)
                sp.sem_inc(M["sent"], 1)
            sp.wait_ge(M["out"], 16 * G4)

        @block.tensor
        def _(pe):
            pe.wait_ge(tok_in, 16 * 4)
            for o in range(2):
                for c in range(8):
                    mm = pe.matmul(ps[6 + o][:, 64 * c:64 * c + 64], c_cols[:, o, c, :], tok_w[:], start=True, stop=True)
                mm.then_inc(mapw_ps, 1)

            def rows_of(u):
                pe.wait_ge(x_in[u], 16)
                for q in range(16):
                    for high in range(2):
                        mm = pe.matmul(ps[u][64 * high:64 * high + 64, 32 * q:32 * q + 32], x_all[:, 16 * u + q, :],
                                       c_rows[:, 32 * high:32 * high + 32], start=True, stop=True)
                mm.then_inc(rowed_ps, 1)

            def columns_of(u):
                if u == 0:
                    pe.wait_ge(mapw_sb, 2)
                pe.wait_ge(rowed_sb, u // 2 + 1)
                if u >= 2:
                    pe.wait_ge(tok_sb, u - 1)
                for o in range(2):
                    mm = pe.matmul(ps[4 + u % 2], rowed[:, o, 8 * u:8 * u + 8, :].rearrange("p q r -> p (q r)"),
                                   mapw[:, o, :], start=(o == 0), stop=(o == 1))
                mm.then_inc(tok_ps, 1)

            rows_of(0)
            for u in range(4):
                if u < 3:
                    rows_of(u + 1)
                columns_of(2 * u)
                columns_of(2 * u + 1)
            pe.wait_ge(attn_in, ATTN_IN)
            pe.sem_inc(B["xs_free"], 1)
            with pe.Fori(0, G8) as g:
                pe.wait_ge(B["xs"], g + 1)
                pe.matmul(ps[0], wk_bd[:], xs8[:], start=True, stop=True).then_inc(B["k_ps"], 1)
                for u in range(4):
                    mm = pe.matmul(ps[1 + u // 2][:, 256 * (u % 2):256 * (u % 2) + 256], xs8[:, P * u:P * u + P],
                                   wqv_bd[:].rearrange("p a b -> p (a b)"), start=True, stop=True)
                    if u % 2:
                        mm.then_inc(B["qv_ps"], 1)
                pe.wait_ge(B["kexp"], g + 1)
                for u in range(4):
                    mm = pe.transpose(ps[3][:, P * u:P * u + P], kexp[:, 2 * u:2 * u + 2, :].rearrange("p a b -> p (a b)"),
                                      ident[:])
                mm.then_inc(B["kT_ps"], 1)
                pe.wait_ge(B["qnorm"], g + 1)
                for u in range(4):
                    mm = pe.transpose(ps[4][:, P * u:P * u + P], qv[:, u, 0, :], ident[:])
                mm.then_inc(B["qT_ps"], 1)
                pe.wait_ge(B["kT_sb"], 2 * g + 2)
                for j in range(8):
                    mm = pe.matmul(ps[5 + j // 4][:, P * (j % 4):P * (j % 4) + P], kT[:, j % 2, j // 2, :], qv[:, j // 2, 1, :],
                                   start=True, stop=True)
                    if j % 4 == 3:
                        mm.then_inc(B["ctx_ps"], 1)
                pe.wait_ge(B["qT_sb"], g + 1)
                pe.wait_ge(B["ctx_sb"], g + 1)
                for j in range(8):
                    mm = pe.matmul(ps[7][:, 64 * j:64 * j + 64], ctx_bd[:, j, :], qT[:, 64 * j:64 * j + 64],
                                   start=True, stop=True)
                mm.then_inc(B["att_ps"], 1)
                pe.wait_ge(B["att_sb"], g + 1)
                pe.matmul(ps[0], wr_bd[:], att_sb[:], start=True, stop=True).then_inc(B["out_ps"], 1)
                pe.wait_ge(B["out_sb"], g + 1)
                pe.sem_inc(B["xs_free"], 1)

            pe.wait_ge(moe_in, MOE_IN)
            pe.wait_ge(w12_ready, 2)
            pe.wait_ge(pads, PADS)

            def moe_turn(g):
                pe.wait_ge(C["xs"], g + 1)
                for j in range(4):
                    m = D if j else P
                    mm = pe.transpose(ps[6][0:m, P * j:P * j + P], xs4[:, D * j:D * j + m], ident[:])
                mm.then_inc(C["xT_ps"], 1)

            def moe_gate(g):
                pe.wait_ge(C["xT_sb"], g + 1)
                for j in range(4):
                    mm = pe.matmul(ps[7][:, 16 * j:16 * j + 16], xT4[:, P * j:P * j + P], gate[:], start=True, stop=True)
                mm.then_inc(C["logit_ps"], 1)

            def moe_down(g, e, first):
                k = e // 2
                pe.wait_ge(C["hid"], 16 * g + e + 1)
                if e % 2 == 0 and not (first and k < 2):
                    pe.wait_ge(C["yw"], 8 * g + k - 1)
                for j in range(4):
                    mm = pe.matmul(ps[4 + k % 2][:, 256 * (e % 2) + D * j:256 * (e % 2) + D * j + D],
                                   hid[:, e % 2, P * j:P * j + P], w3[:, e, :], start=True, stop=True)
                mm.then_inc(C["y_ps"], 1)

            def moe_group(g, b, first):
                pe.wait_ge(C["xh"], g + 1)
                pe.wait_ge(C["xl"], g + 1)
                for e in range(EXPERTS):
                    if not (first and e < 2):
                        pe.wait_ge(C["silu"], 16 * g + e - 1)
                    for n, done in enumerate(("h1_ps", "h2_ps")):
                        if n and not (first and e < 2):
                            pe.wait_ge(C["hid"], 16 * g + e - 1)
                        pe.matmul(ps[2 * n + e % 2], w12_hi[:, n, e, :], x2[:, b, :], start=True, stop=False)
                        pe.matmul(ps[2 * n + e % 2], w12_lo[:, n, e, :], x2[:, b, :], start=False, stop=True).then_inc(C[done], 1)
                    if e > 0:
                        moe_down(g, e - 1, first)
                    if e == 1:
                        moe_turn(g + 1)
                    if e == 3:
                        moe_gate(g + 1)
                moe_down(g, EXPERTS - 1, first)

            moe_turn(0)
            moe_gate(0)
            for b in range(2):
                moe_group(b, b, b == 0)
            with pe.Fori(1, G4 // 2) as i:
                for b in range(2):
                    moe_group(2 * i + b, b, False)

            pe.wait_ge(l1_in, L1_IN)
            pe.wait_ge(C["acc"], 15 * G4)

            def turn(p):
                pe.wait_ge(X["xs"], p + 1)
                pe.transpose(ps[4][:, 0:P], xs1[:], ident[:]).then_inc(X["xT_ps"], 1)

            def queries(p):
                pe.wait_ge(X["xTq"], 2 * p + 2)
                pe.matmul(ps[5], xTq[:], wqv[:, 0:QK], start=True, stop=True).then_inc(X["q_ps"], 1)

            def values_b(p, b):
                pe.wait_ge(X["qd"], p + 1)
                pe.wait_ge(X["xT_sb"], p + 1)
                pe.matmul(ps[5], xT1[:, b, :], wqv[:, 2 * QK:3 * QK], start=True, stop=True).then_inc(X["vb_ps"], 1)

            def values_f(p, b, image, odd, first):
                if image == 0 and odd == 0 and not first:
                    pe.wait_ge(X["attq"], p - 1)
                w = wqv[:, QK:2 * QK].rearrange("k (n o d) -> k n o d", o=2, d=D)[:, :, odd, :]
                mm = pe.matmul(ps[6][64 * odd:64 * odd + 64, 256 * image:256 * image + 256], xT1[:, b, 64 * image:64 * image + 64],
                               w, start=True, stop=True)
                if image and odd:
                    mm.then_inc(X["vf_ps"], 1)

            def turn_attn(p):
                pe.wait_ge(X["attk"], p + 1)
                pe.wait_ge(X["vf"], p + 1)
                for n in range(4):
                    mm = pe.transpose(ps[6][:, P * n:P * n + P], attk[:, 2 * n:2 * n + 2, :].rearrange("p h s -> p (h s)"), ident[:])
                mm.then_inc(X["attq_ps"], 1)

            def attend(p, b, image, part):
                if image == 0 and part == 0:
                    pe.wait_ge(X["attq"], p + 1)
                    pe.wait_ge(X["vb"], p + 1)
                at = slice(64 * image, 64 * image + 64)
                if part == 0:
                    for n in range(4):
                        pe.matmul(ps[7][at, 0:D], attq[:, n, at], vf[:, b, image, n, :], start=(n == 0), stop=False)
                    return
                for n in range(4 * part - 4, 4 * part):
                    mm = pe.matmul(ps[7][at, 0:D], attk[at, n, :], vb[at, b, n, :], start=False, stop=(n == HEADS - 1))
                if image == 1 and part == 2:
                    mm.then_inc(X["o_ps"], 1)

            def turn_y(p):
                pe.wait_ge(X["y"], p + 1)
                pe.transpose(ps[7][:, 128:128 + P], osb[:, 2:4, :].rearrange("p a d -> p (a d)"), ident[:]).then_inc(X["yT_ps"], 1)

            def fan_in(p):
                pe.wait_ge(X["yT"], p + 1)
                pe.matmul(ps[7][:, 64:128], yT[:], fan[:], start=True, stop=True).then_inc(X["fan_ps"], 1)

            def pair(p, b, first):
                for k in range(32):
                    image, blk, t = k // 16, k % 16 // 4, k % 4
                    if k % 16 == 0:
                        pe.wait_ge(X[f"tb{image}"], 16 * 8 * (p + 1))
                    if k >= 2 and k - 2 in POOLED:
                        pe.wait_ge(X["abs"], len(POOLED) * p + POOLED.index(k - 2) + 1)
                    elif k >= 2:
                        pe.wait_ge(X["red"], len(REDUCED) * p + REDUCED.index(k - 2) + 1)
                    elif not first:
                        pe.wait_ge(X["red"], len(REDUCED) * p + k - 1)
                    for n in range(2):
                        mm = pe.matmul(ps[2 * (k % 2) + n], pick[:, 2 * t + n, :], blocks[:, image, blk // 2, blk % 2, :],
                                       start=True, stop=True)
                    mm.then_inc(X["diff"], 1)
                    if k == 2:
                        turn(p + 1)
                    if k == 5:
                        queries(p + 1)
                    if not first:
                        if k == 10:
                            turn_attn(p - 1)
                        if 12 <= k < 18:
                            attend(p - 1, 1 - b, (k - 12) // 3, (k - 12) % 3)
                        if k == 21:
                            turn_y(p - 1)
                        if k == 24:
                            fan_in(p - 1)
                    if k == 25:
                        values_b(p + 1, 1 - b)
                    if 26 <= k < 30:
                        values_f(p + 1, 1 - b, (k - 26) // 2, k % 2, first)

            turn(0)
            queries(0)
            values_b(0, 0)
            for n in range(4):
                values_f(0, 0, n // 2, n % 2, True)
            pair(0, 0, True)
            pair(1, 1, False)
            with pe.Fori(1, PAIRS // 2) as i:
                for b in range(2):
                    pair(2 * i + b, b, False)
            turn_attn(PAIRS - 1)
            for n in range(6):
                attend(PAIRS - 1, 1, n // 3, n % 3)
            turn_y(PAIRS - 1)
            fan_in(PAIRS - 1)

            pe.wait_ge(mlp_in, MLP_IN)
            pe.wait_ge(X["sum"], PAIRS)
            pe.wait_ge(pads, PADS + 2)
            pe.sem_inc(M["free"], 1)
            with pe.Fori(0, G4 // 2) as i:
                for b in range(2):
                    pe.wait_ge(M["xs"], 2 * i + b + 1)
                    for j in range(4):
                        m = D if j else P
                        mm = pe.transpose(ps[4 * b][0:m, P * j:P * j + P], xs5[:, b, D * j:D * j + m], ident[:])
                    mm.then_inc(M["xT_ps"], 1)
                for b in range(2):
                    pe.wait_ge(M["xT"], 2 * i + b + 1)
                    pe.matmul(ps[4 * b + 1], wi[:], xT5[:, b, :], start=True, stop=True).then_inc(M["h0_ps"], 1)
                for l in range(2):
                    for b in range(2):
                        pe.wait_ge(M[f"h{l}"], (1, 4)[l] * (2 * i + b + 1))
                        pe.wait_ge(M[f"sel{l}"], 2 * i + b + 1)
                        for j in range(4):
                            mm = pe.matmul(ps[4 * b + 2 + l][:, P * j:P * j + P], wsel[:, l, b, j, 0:HID],
                                           hm[:, l, b, P * j:P * j + P], start=True, stop=True)
                        mm.then_inc(M[f"h{l + 1}_ps"], 1)
                for b in range(2):
                    pe.wait_ge(M["h2"], 4 * (2 * i + b + 1))
                    for j in range(4):
                        mm = pe.matmul(ps[4 * b][:, D * j:D * j + D], hm[:, 2, b, P * j:P * j + P], wo[:], start=True, stop=True)
                    mm.then_inc(M["o_ps"], 1)
                pe.wait_ge(M["fin"], 2 * i + 2)
                pe.sem_inc(M["free"], 1)

        @block.scalar
        def _(act):
            act.dma_start(c_cols[:].rearrange("p a b c -> p (a b c)"), a["c_cols"]).then_inc(tok_in, 16)
            act.dma_start(tok_w[:], a["L0_tok_W"]).then_inc(tok_in, 16)
            act.dma_start(c_rows[:], a["c_rows"]).then_inc(tok_in, 16)
            act.dma_start(tok_b[:], a["L0_tok_b"].partition_broadcast(P)).then_inc(tok_in, 16)
            for o in range(2):
                act.wait_ge(mapw_ps, o + 1)
                nc.scalar.copy(mapw[:, o, :], ps[6 + o]).then_inc(mapw_sb, 1)
            for u in range(4):
                act.wait_ge(rowed_ps, u + 1)
                nc.scalar.copy(rowed[:, :, 16 * u:16 * u + 16, :].rearrange("p o q r -> p q o r"),
                               ps[u].rearrange("p (q o r) -> p q o r", q=16, o=2)).then_inc(rowed_sb, 1)
            layernorm_act(act, 0)
            act.wait_ge(attn_in, ATTN_IN)
            with act.Fori(0, G8) as g:
                act.wait_ge(B["k_ps"], g + 1)
                nc.scalar.activation(kexp[:].rearrange("p a b -> p (a b)"), ps[0], ACT.Identity,
                                     bias=bk2[:, 0:1]).then_inc(B["k_sb"], 1)
                act.wait_ge(B["kcen"], g + 1)
                nc.scalar.activation(kexp[:], kexp[:], ACT.Exp).then_inc(B["kexp"], 1)
                act.wait_ge(B["qcen"], g + 1)
                nc.scalar.activation(qv[:, :, 0, :], qv[:, :, 0, :], ACT.Exp).then_inc(B["qexp"], 1)
                act.wait_ge(B["kT_ps"], g + 1)
                for b in range(2):
                    half = slice(64 * b, 64 * b + 64)
                    nc.scalar.copy(kT[half, b, :, :].rearrange("p a b -> p (a b)"), ps[3][half, :]).then_inc(B["kT_sb"], 1)
                act.wait_ge(B["qT_ps"], g + 1)
                nc.scalar.copy(qT[:], ps[4]).then_inc(B["qT_sb"], 1)
                act.wait_ge(B["att_ps"], g + 1)
                nc.scalar.copy(att_sb[:], ps[7]).then_inc(B["att_sb"], 1)

            layernorm_act(act, 1)
            act.wait_ge(w12_in, 16 * 4)
            nc.scalar.activation(w12_hi[:].rearrange("p w e n -> p (w e n)"), big2[:, 0:PAIRS * D], ACT.Copy, scale=W_SCALE).then_inc(w12_ready, 1)

            def moe_x(g, b):
                act.wait_ge(C["xT_ps"], g + 1)
                act.wait_ge(C["logit_ps"], g)
                nc.scalar.copy(xT4[0:D, :], ps[6][0:D, :]).then_inc(C["xT_sb"], 1)
                nc.scalar.copy(x2[0:D, b, :], ps[6][0:D, :]).then_inc(C["xh"], 1)

            def moe_group(g, b, first):
                for e in range(EXPERTS):
                    act.wait_ge(C["h1_ps"], 16 * g + e + 1)
                    if not (first and e < 2):
                        act.wait_ge(C["hid"], 16 * g + e - 1)
                    nc.scalar.activation(silu[:, e % 2, :], ps[e % 2], ACT.Silu, scale=1.0 / W_SCALE).then_inc(C["silu"], 1)
                    if e == 2:
                        moe_x(g + 1, 1 - b)
                    if e == 13:
                        act.wait_ge(C["gap"], g + 2)
                        nc.scalar.activation(gst[:, 5, :], gst[:, 4, :], ACT.Tanh, scale=0.5).then_inc(C["tanh"], 1)

            moe_x(0, 0)
            act.wait_ge(C["gap"], 1)
            nc.scalar.activation(gst[:, 5, :], gst[:, 4, :], ACT.Tanh, scale=0.5).then_inc(C["tanh"], 1)
            for b in range(2):
                moe_group(b, b, b == 0)
            with act.Fori(1, G4 // 2) as i:
                for b in range(2):
                    moe_group(2 * i + b, b, False)

            layernorm_act(act, 2)

            def prepare_x(p, b):
                act.wait_ge(X["xT_ps"], p + 1)
                nc.scalar.copy(xT1[0:D, b, :], ps[4][0:D, 0:P]).then_inc(X["xT_sb"], 1)
                act.wait_ge(X["q_ps"], p)
                for image in range(2):
                    at = slice(64 * image, 64 * image + 64)
                    nc.scalar.copy(xTq[0:D, at].rearrange("d (i x t) -> d x i t", i=2, x=4),
                                   ps[4][0:D, at].rearrange("d (x i t) -> d x i t", x=4, i=2)).then_inc(X["xTq"], 1)

            def high_q(p):
                act.wait_ge(X["q_ps"], p + 1)
                nc.scalar.copy(qk[:, 0, 0, :], ps[5]).then_inc(X["qh"], 1)

            def low_q(p):
                act.wait_ge(X["qd"], p + 1)
                nc.scalar.activation(qk[:, 0, 1, :], lo_f[:, 0, :], ACT.Copy, scale=LO_SCALE).then_inc(X["ql"], 1)

            def high_k(p):
                act.wait_ge(X["kf"], p + 1)
                act.wait_ge(X["tb0"], 16 * 8 * p)
                act.wait_ge(X["tb1"], 16 * 8 * p)
                nc.scalar.copy(qk[:, 1, 0, :], kf[:].rearrange("p h d -> p (h d)")).then_inc(X["kh"], 1)

            def low_k(p):
                act.wait_ge(X["kd"], p + 1)
                nc.scalar.activation(qk[:, 1, 1, :], lo_f[:, 1, :], ACT.Copy, scale=LO_SCALE).then_inc(X["kl"], 1)

            def exponentials(p, image, first):
                act.wait_ge(X["red"], len(REDUCED) * p + (image + 1) * len(REDUCED) // 2)
                act.wait_ge(X["pooled"], len(POOLED) * p + (image + 1) * len(POOLED) // 2)
                if not first:
                    act.wait_ge(X["attk"], p)
                    act.wait_ge(X["attn"], 16 * 16 * p)
                nc.scalar.activation(expd[:, image, :], score[:, image].rearrange("p j i t h -> p (j i t h)"), ACT.Exp,
                                     scale=-(float(D) ** -0.5)).then_inc(X["exp"], 1)

            def turned_attn(p):
                act.wait_ge(X["attq_ps"], p + 1)
                nc.scalar.copy(attq[:].rearrange("p a b -> p (a b)"), ps[6]).then_inc(X["attq"], 1)

            def gate_o(p):
                act.wait_ge(X["o_ps"], p + 1)
                nc.scalar.activation(osb[:, 0, :], ps[7][:, 0:D], ACT.Exp, scale=-1.702).then_inc(X["sig"], 1)

            def turned_y(p):
                act.wait_ge(X["yT_ps"], p + 1)
                nc.scalar.copy(yT[0:D, :], ps[7][0:D, 128:128 + P]).then_inc(X["yT"], 1)

            def values(p, b, first):
                act.wait_ge(X["vb_ps"], p + 1)
                if not first:
                    act.wait_ge(X["o_ps"], p - 1)
                nc.scalar.copy(vb[:, b].rearrange("p h d -> p (h d)"), ps[5]).then_inc(X["vb"], 1)
                act.wait_ge(X["vf_ps"], p + 1)
                nc.scalar.copy(vf[:, b].rearrange("p i n d -> p (i n d)"), ps[6]).then_inc(X["vf"], 1)

            def absolute(p, k, first):
                n = POOLED.index(k)
                act.wait_ge(X["diff"], 32 * p + k + 1)
                if not (first and n < 2):
                    act.wait_ge(X["pooled"], len(POOLED) * p + n - 1)
                nc.scalar.activation(absd[:, n % 2], pp[:, 2 * (k % 2):2 * (k % 2) + 2, :].rearrange("p n (h w) -> p (n h) w", w=D),
                                     ACT.Abs).then_inc(X["abs"], 1)

            def pair(p, b, first):
                absolute(p, 1, first)
                prepare_x(p + 1, 1 - b)
                absolute(p, 4, first)
                high_k(p + 1)
                high_q(p + 1)
                absolute(p, 7, first)
                absolute(p, 10, first)
                low_q(p + 1)
                low_k(p + 1)
                if not first:
                    turned_attn(p - 1)
                exponentials(p, 0, first)
                absolute(p, 17, first)
                if not first:
                    gate_o(p - 1)
                absolute(p, 20, first)
                if not first:
                    turned_y(p - 1)
                absolute(p, 23, first)
                absolute(p, 26, first)
                values(p + 1, 1 - b, first)
                exponentials(p, 1, first)

            act.wait_ge(pads, PADS)
            prepare_x(0, 0)
            high_k(0)
            high_q(0)
            low_q(0)
            low_k(0)
            values(0, 0, True)
            pair(0, 0, True)
            pair(1, 1, False)
            with act.Fori(1, PAIRS // 2) as i:
                for b in range(2):
                    pair(2 * i + b, b, False)
            turned_attn(PAIRS - 1)
            gate_o(PAIRS - 1)
            turned_y(PAIRS - 1)

            layernorm_act(act, 3)
            with act.Fori(0, G4 // 2) as i:
                for b in range(2):
                    act.wait_ge(M["xT_ps"], 2 * i + b + 1)
                    nc.scalar.copy(xT5[0:D, b, :], ps[4 * b][0:D, :]).then_inc(M["xT"], 1)
                for b in range(2):
                    act.wait_ge(M["h0_ps"], 2 * i + b + 1)
                    nc.scalar.activation(hm[:, 0, b, :], ps[4 * b + 1], ACT.Relu).then_inc(M["h0"], 1)
                for l in range(2):
                    for b in range(2):
                        act.wait_ge(M[f"h{l + 1}_ps"], 2 * i + b + 1)
                        for j in range(4):
                            nc.scalar.activation(hm[:, l + 1, b, P * j:P * j + P], ps[4 * b + 2 + l][:, P * j:P * j + P], ACT.Relu,
                                                 bias=wsel[:, l, b, j, HID:HID + 1]).then_inc(M[f"h{l + 1}"], 1)

        @block.vector
        def _(dve):
            dve.memset(kT[:], 0.0)
            dve.memset(xs1[:], 0.0).then_inc(pads, 1)
            dve.memset(xn[:, PAIRS:, :], 0.0).then_inc(pads, 1)
            for t in (xT4[D:KA, :], xT1[D:KA], xTq[D:KA, :], yT[D:KA, :], gate[D:KA, :], wqv[D:KA, :], fan[D:KA, :], wi[D:KA, :]):
                dve.memset(t, 0.0).then_inc(pads, 1)
            dve.wait_ge(pads, 10)
            for t in (xT4[D:D + 1, :], xT1[D:D + 1], xTq[D:D + 1, :], yT[D:D + 1, :]):
                dve.memset(t, 1.0).then_inc(pads, 1)
            dve.memset(wk_bd[:], 0.0)
            dve.memset(wqv_bd[:], 0.0)
            dve.memset(wr_bd[:], 0.0).then_inc(zeroed, 1)

            dve.wait_ge(tok_in, 16 * 4)
            for u in range(8):
                dve.wait_ge(tok_ps, u + 1)
                dve.tensor_tensor(tok_rows[:, u, :].rearrange("p (c d) -> p c d", d=D),
                                  ps[4 + u % 2].rearrange("p (c d) -> p c d", d=D),
                                  tok_b[:].unsqueeze(1).to_broadcast([P, 8, D]), ALU.add).then_inc(tok_sb, 1)

            dve.wait_ge(h_in, 16)
            dve.wait_ge(tok_out, 16 * 8)
            layernorm_dve(dve, 0)
            dve.wait_ge(attn_in, ATTN_IN)
            with dve.Fori(0, G8) as g:
                kmax, ksum, krec = (kst[:, n, :] for n in range(3))
                dve.wait_ge(B["k_sb"], g + 1)
                dve.tensor_reduce(kmax, kexp[:], AX.X, ALU.max).then_inc(B["kmax"], 1)
                dve.wait_ge(B["kmax"], g + 1)
                dve.tensor_tensor(kexp[:], kexp[:], kmax.unsqueeze(2).to_broadcast([P, 8, D]),
                                  ALU.subtract).then_inc(B["kcen"], 1)
                for u in range(2):
                    dve.wait_ge(B["qv_ps"], 2 * g + u + 1)
                    dve.tensor_tensor(qv[:, 2 * u:2 * u + 2, :, :].rearrange("p u a m -> p u (a m)"),
                                      ps[1 + u].rearrange("p (u n) -> p u n", u=2),
                                      bqv[:].rearrange("p a b d -> p (a b d)").unsqueeze(1).to_broadcast([P, 2, 256]),
                                      ALU.add).then_inc(B["qv_sb"], 1)
                qq = qv[:, :, 0, :].rearrange("p u (n k) -> p u n k", k=8)
                qmax, qsum, qrec = (qst[:, n, :, :] for n in range(3))
                spread = [P, 4, 16, 8]
                dve.wait_ge(B["qv_sb"], 2 * g + 2)
                dve.tensor_reduce(qmax, qq, AX.X, ALU.max).then_inc(B["qmax"], 1)
                dve.wait_ge(B["qmax"], g + 1)
                dve.tensor_tensor(qq, qq, qmax.unsqueeze(3).to_broadcast(spread), ALU.subtract).then_inc(B["qcen"], 1)
                dve.wait_ge(B["kexp"], g + 1)
                dve.tensor_reduce(ksum, kexp[:], AX.X, ALU.add).then_inc(B["ksum"], 1)
                dve.wait_ge(B["ksum"], g + 1)
                dve.reciprocal(krec, ksum).then_inc(B["krec"], 1)
                dve.wait_ge(B["qexp"], g + 1)
                dve.tensor_reduce(qsum, qq, AX.X, ALU.add).then_inc(B["qsum"], 1)
                dve.wait_ge(B["qsum"], g + 1)
                dve.reciprocal(qrec, qsum).then_inc(B["qrec"], 1)
                dve.wait_ge(B["qrec"], g + 1)
                dve.tensor_tensor(qq, qq, qrec.unsqueeze(3).to_broadcast(spread), ALU.mult).then_inc(B["qnorm"], 1)
                dve.wait_ge(B["krec"], g + 1)
                for j in range(8):
                    if j % 4 == 0:
                        dve.wait_ge(B["ctx_ps"], 2 * g + j // 4 + 1)
                    op = dve.scalar_tensor_tensor(out=ctx_bd[:, j, :], in0=ps[5 + j // 4][:, P * (j % 4):P * (j % 4) + P],
                                                  scalar=krec[:, j:j + 1], in1=same_head[:], op0=ALU.mult, op1=ALU.mult)
                op.then_inc(B["ctx_sb"], 1)
                dve.wait_ge(B["out_ps"], g + 1)
                hg = h[:, bass.ts(g, 8), :]
                dve.scalar_tensor_tensor(out=hg, in0=ps[0].rearrange("p (n d) -> p n d", d=D), scalar=br2[:, 0:1],
                                         in1=hg, op0=ALU.add, op1=ALU.add).then_inc(B["out_sb"], 1)

            dve.wait_ge(B["out_sb"], G8)
            layernorm_dve(dve, 1)
            dve.wait_ge(w12_ready, 1)
            dve.scalar_tensor_tensor(out=w12_lo[:].rearrange("p w e n -> p (w e n)"), in0=big2[:, 0:PAIRS * D], scalar=W_SCALE,
                                     in1=w12_hi[:].rearrange("p w e n -> p (w e n)"), op0=ALU.mult,
                                     op1=ALU.subtract).then_inc(w12_ready, 1)
            dve.wait_ge(moe_in, MOE_IN)
            GATE = 14
            spread = [P, 4, EXPERTS]

            def low_x(g, b):
                dve.wait_ge(C["xh"], g + 1)
                dve.tensor_tensor(x2[D:P, b, :], ps[6][0:D, :], x2[0:D, b, :], ALU.subtract).then_inc(C["xl"], 1)

            def gating(g, b):
                m1, m2, r1, r2 = (gst[:, n, :] for n in range(4))
                gap, th = gst[:, 4, :], gst[:, 5, :]
                one, two, t = (gsc[:, n, :, :] for n in range(3))
                ranks = rank[:].unsqueeze(1).to_broadcast(spread)
                n = [0]

                def after(ins):
                    n[0] += 1
                    ins.then_inc(C["gate"], 1)
                    dve.wait_ge(C["gate"], GATE * g + n[0])

                def wide(v):
                    return v.unsqueeze(2).to_broadcast(spread)

                dve.wait_ge(C["logit_ps"], g + 1)
                after(dve.tensor_copy(logit[:].rearrange("p j e -> p (j e)"), ps[7][:, 0:64]))
                after(dve.tensor_reduce(m1, logit[:], AX.X, ALU.max))
                yield
                after(dve.tensor_tensor(t, logit[:], wide(m1), ALU.is_equal))
                after(dve.tensor_tensor(t, t, ranks, ALU.mult))
                yield
                after(dve.tensor_reduce(r1, t, AX.X, ALU.max))
                after(dve.tensor_tensor(one, t, wide(r1), ALU.is_equal))
                yield
                after(dve.scalar_tensor_tensor(out=two, in0=one, scalar=-1e30, in1=logit[:], op0=ALU.mult, op1=ALU.add))
                after(dve.tensor_reduce(m2, two, AX.X, ALU.max))
                yield
                dve.tensor_tensor(gap, m2, m1, ALU.subtract).then_inc(C["gap"], 1)
                after(dve.tensor_tensor(t, two, wide(m2), ALU.is_equal))
                after(dve.tensor_tensor(t, t, ranks, ALU.mult))
                yield
                after(dve.tensor_reduce(r2, t, AX.X, ALU.max))
                after(dve.tensor_tensor(two, t, wide(r2), ALU.is_equal))
                yield
                yield
                dve.wait_ge(C["tanh"], g + 1)
                after(dve.tensor_tensor(t, one, two, ALU.subtract))
                after(dve.tensor_tensor(t, t, wide(th), ALU.mult))
                yield
                dve.tensor_tensor(one, one, two, ALU.add).then_inc(C["disp"], 1)
                dve.wait_ge(C["disp"], 3 * g + 1)
                dve.tensor_tensor(one, one, t, ALU.subtract).then_inc(C["disp"], 1)
                dve.wait_ge(C["disp"], 3 * g + 2)
                dve.tensor_scalar(disp[:, b, :, :], one, 0.5, None, ALU.mult).then_inc(C["disp"], 1)
                assert n[0] == GATE
                yield

            def weigh(g, b, k, first):
                dve.wait_ge(C["y_ps"], 16 * g + 2 * k + 2)
                if k == 0:
                    dve.wait_ge(C["disp"], 3 * g + 3)
                if not (first and k < 2):
                    dve.wait_ge(C["acc"], ACC(8 * g + k - 2, g, k - 2))
                dve.tensor_tensor(yw[:, k % 2].rearrange("p e (j o) -> p e j o", j=4),
                                  ps[4 + k % 2].rearrange("p (e j o) -> p e j o", e=2, j=4),
                                  disp[:, b, :, 2 * k:2 * k + 2].rearrange("p j e -> p e j").unsqueeze(3).to_broadcast([P, 2, 4, D]),
                                  ALU.mult).then_inc(C["yw"], 1)

            def moe_group(g, b, first):
                gates = None
                for e in range(EXPERTS):
                    dve.wait_ge(C["h2_ps"], 16 * g + e + 1)
                    dve.wait_ge(C["silu"], 16 * g + e + 1)
                    if not (first and e < 2):
                        dve.wait_ge(C["y_ps"], 16 * g + e - 1)
                    dve.scalar_tensor_tensor(out=hid[:, e % 2, :], in0=ps[2 + e % 2], scalar=1.0 / W_SCALE,
                                             in1=silu[:, e % 2, :], op0=ALU.mult, op1=ALU.mult).then_inc(C["hid"], 1)
                    if e >= 2 and e % 2 == 0:
                        weigh(g, b, e // 2 - 1, first)
                    if e == 3:
                        low_x(g + 1, 1 - b)
                    if e == 5:
                        gates = gating(g + 1, 1 - b)
                    if e >= 6 and gates is not None:
                        next(gates, None)
                weigh(g, b, 7, first)
                for _ in gates:
                    pass

            low_x(0, 0)
            for _ in gating(0, 0):
                pass
            for b in range(2):
                moe_group(b, b, b == 0)
            with dve.Fori(1, G4 // 2) as i:
                for b in range(2):
                    moe_group(2 * i + b, b, False)

            dve.wait_ge(C["sum"], G4)
            layernorm_dve(dve, 2)

            def low_q(p):
                dve.wait_ge(X["qh"], p + 1)
                dve.wait_ge(X["ql"], p)
                dve.tensor_tensor(lo_f[:, 0, :], ps[5], qk[:, 0, 0, :], ALU.subtract).then_inc(X["qd"], 1)

            def key_sums(p):
                z, z1, zr = (zst[:, n, :] for n in range(3))
                dve.wait_ge(X["attn"], 16 * 16 * (p + 1))
                dve.tensor_reduce(z, attn[:].rearrange("p s h -> p h s"), AX.X, ALU.add).then_inc(X["z"], 1)
                dve.wait_ge(X["z"], p + 1)
                dve.tensor_scalar(z1, z, 1.0, None, ALU.add).then_inc(X["z1"], 1)
                dve.wait_ge(X["z1"], p + 1)
                dve.reciprocal(zr, z1).then_inc(X["zr"], 1)

            def gate_o(p):
                dve.wait_ge(X["sig"], p + 1)
                dve.tensor_scalar(osb[:, 1, :], osb[:, 0, :], 1.0, None, ALU.add).then_inc(X["den"], 1)
                dve.wait_ge(X["den"], p + 1)
                dve.reciprocal(osb[:, 3, :], osb[:, 1, :]).then_inc(X["rden"], 1)
                dve.wait_ge(X["rden"], p + 1)
                dve.tensor_tensor(osb[:, 2, :], ps[7][:, 0:D], osb[:, 3, :], ALU.mult).then_inc(X["y"], 1)

            def finish(p, slot):
                dve.wait_ge(X["fan_ps"], p + 1)
                dve.wait_ge(X["hx"], p + 1)
                dve.tensor_tensor(h[:, slot, :], ps[7][:, 64:128], hx[:], ALU.add).then_inc(X["sum"], 1)

            def pair(p, b, slot, first):
                for k in range(32):
                    image, blk, t = k // 16, k % 16 // 4, k % 4
                    if k not in POOLED:
                        dve.wait_ge(X["diff"], 32 * p + k + 1)
                        if k % 16 == 0 and not first:
                          dve.wait_ge(X["exp"], 2 * p + image - 1)
                        dve.tensor_reduce(score[:, image, blk // 2, blk % 2, 2 * t:2 * t + 2, :].rearrange("p t h -> p (t h)"),
                                        pp[:, 2 * (k % 2):2 * (k % 2) + 2, :].rearrange("p n (h w) -> p (n h) w", w=D), AX.X, ALU.add,
                                        apply_absolute_value=True).then_inc(X["red"], 1)
                    if k == 8:
                        low_q(p + 1)
                    if not first:
                        if k == 3:
                            key_sums(p - 1)
                        if k == 19:
                            gate_o(p - 1)
                        if k == 28:
                            finish(p - 1, slot)

            low_q(0)
            pair(0, 0, None, True)
            pair(1, 1, slice(0, 1), False)
            with dve.Fori(1, PAIRS // 2) as i:
                for b in range(2):
                    pair(2 * i + b, b, bass.ds(2 * i + b - 1, 1), False)
            key_sums(PAIRS - 1)
            gate_o(PAIRS - 1)
            finish(PAIRS - 1, slice(PAIRS - 1, PAIRS))

            dve.wait_ge(X["sum"], PAIRS)
            layernorm_dve(dve, 3)
            dve.memset(xT5[D:KA], 0.0).then_inc(pads, 1)
            dve.wait_ge(pads, PADS + 1)
            dve.memset(xT5[D:D + 1], 1.0).then_inc(pads, 1)
            dve.wait_ge(mlp_in, MLP_IN)
            for l in range(2):
                dve.tensor_tensor(ws[:, l, 0:HID], ws[:, l, 0:HID], ident[:], ALU.add).then_inc(wc_ready, 1)
            dve.wait_ge(wc_ready, 2)
            for l in range(2):
                dve.tensor_tensor(wc[:, l], wc[:, l], ws[:, l, :].unsqueeze(1).to_broadcast([P, EXPERTS, HID + 1]),
                                  ALU.add).then_inc(wc_ready, 1)
            dve.wait_ge(wc_ready, 4)
            with dve.Fori(0, G4 // 2) as i:
                for b in range(2):
                    for j in range(4):
                        r = dve.value_load(route[0:1, bass.ds(8 * i + 4 * b + j, 1)], min_val=0, max_val=EXPERTS - 1)
                        for l in range(2):
                            op = dve.tensor_copy(wsel[:, l, b, j, :].unsqueeze(1), wc[:, l, bass.ds(r, 1), :])
                            if j == 3:
                                op.then_inc(M[f"sel{l}"], 1)
                for b in range(2):
                    dve.wait_ge(M["o_ps"], 2 * i + b + 1)
                    dve.wait_ge(M["hb"], 2 * i + b + 1)
                    dve.wait_ge(M["sent"], i + 1)
                    dve.tensor_tensor(fin[:, b, :], ps[4 * b][:, 0:4 * D], hb[:, b, :], ALU.add).then_inc(M["fin"], 1)

        @block.gpsimd
        def _(pool):
            pool.wait_ge(xn_ready[0], 1)
            with pool.Fori(0, G8) as g:
                pool.wait_ge(B["xs_free"], g + 1)
                nc.gpsimd.tensor_copy(xs8[:].rearrange("p (n d) -> p n d", d=D), xn[:, bass.ts(g, 8), :]).then_inc(B["xs"], 1)

            def load_x(g, at):
                if at is not None:
                    pool.wait_ge(C["xT_ps"], g)
                nc.gpsimd.tensor_copy(xs4[:].rearrange("p (n d) -> p n d", d=D), xn[:, at or slice(0, 4), :]).then_inc(C["xs"], 1)

            def moe_group(g, here, following):
                load_x(g + 1, following)
                for k in range(8):
                    pool.wait_ge(C["yw"], 8 * g + k + 1)
                    for n in range(2):
                        if k == 0 and n == 0:
                            pool.wait_ge(C["sum"], g)
                            nc.gpsimd.tensor_tensor(acc[:], yw[:, 0, 0, :], yw[:, 0, 1, :], ALU.add).then_inc(C["acc"], 1)
                        elif k > 0:
                            pool.wait_ge(C["acc"], 15 * g + 2 * k - 1 + n)
                            nc.gpsimd.tensor_tensor(acc[:], acc[:], yw[:, k % 2, n, :], ALU.add).then_inc(C["acc"], 1)
                pool.wait_ge(C["acc"], 15 * g + 15)
                hg = h[:, here, :]
                nc.gpsimd.tensor_tensor(hg, hg, acc[:].rearrange("p (n d) -> p n d", d=D), ALU.add).then_inc(C["sum"], 1)

            pool.wait_ge(xn_ready[1], 1)
            load_x(0, None)
            for b in range(2):
                moe_group(b, slice(4 * b, 4 * b + 4), slice(4 * b + 4, 4 * b + 8))
            with pool.Fori(1, G4 // 2) as i:
                for b in range(2):
                    moe_group(2 * i + b, bass.ds(8 * i + 4 * b, 4), bass.ds(8 * i + 4 * b + 4, 4))

            def load_pair(p, at):
                pool.wait_ge(X["xT_ps"], p)
                pool.wait_ge(X["kf"], p)
                nc.gpsimd.tensor_copy(xs1[:, 0:D].unsqueeze(1), xn[:, at, :]).then_inc(X["xs"], 1)

            def keys(p):
                pool.wait_ge(X["xs"], p + 1)
                pool.wait_ge(X["kh"], p)
                pool.wait_ge(X["kd"], p)
                nc.gpsimd.tensor_tensor(kf[:], xs1[:, 0:D].unsqueeze(1).to_broadcast([P, HEADS, D]), wk_b[:], ALU.mult).then_inc(X["kf"], 1)

            def low_k(p):
                pool.wait_ge(X["kh"], p + 1)
                pool.wait_ge(X["kl"], p)
                nc.gpsimd.tensor_tensor(lo_f[:, 1, :], kf[:].rearrange("p h d -> p (h d)"), qk[:, 1, 0, :],
                                        ALU.subtract).then_inc(X["kd"], 1)

            def normalise(p):
                pool.wait_ge(X["zr"], p + 1)
                pool.wait_ge(X["o_ps"], p)
                nc.gpsimd.tensor_tensor(attk[:].rearrange("p h s -> p s h"), attn[:],
                                        zst[:, 2, :].unsqueeze(1).to_broadcast([P, S, HEADS]), ALU.mult).then_inc(X["attk"], 1)

            def residual(p, at):
                pool.wait_ge(X["sum"], p)
                nc.gpsimd.tensor_tensor(hx[:].unsqueeze(1), h[:, at, :], xn[:, at, :], ALU.add).then_inc(X["hx"], 1)

            def tree(p, k, first):
                n = POOLED.index(k)
                image, blk, t = k // 16, k % 16 // 4, k % 4
                x = absd[:, n % 2]
                pool.wait_ge(X["abs"], len(POOLED) * p + n + 1)
                for m, w in enumerate((32, 16, 8, 4, 2)):
                    if m:
                        pool.wait_ge(X["tree"], 5 * (len(POOLED) * p + n) + m)
                    nc.gpsimd.tensor_tensor(x[:, :, 0:w], x[:, :, 0:w], x[:, :, w:2 * w], ALU.add).then_inc(X["tree"], 1)
                pool.wait_ge(X["tree"], 5 * (len(POOLED) * p + n) + 5)
                if n % (len(POOLED) // 2) == 0 and not first:
                    pool.wait_ge(X["exp"], 2 * p + image - 1)
                nc.gpsimd.tensor_tensor(score[:, image, blk // 2, blk % 2, 2 * t:2 * t + 2, :].rearrange("p t h -> p (t h)").unsqueeze(2),
                                        x[:, :, 0:1], x[:, :, 1:2], ALU.add).then_inc(X["pooled"], 1)

            def pair(p, last, following, first):
                load_pair(p + 1, following)
                tree(p, 1, first)
                keys(p + 1)
                if not first:
                    normalise(p - 1)
                tree(p, 4, first)
                low_k(p + 1)
                tree(p, 7, first)
                tree(p, 10, first)
                if not first:
                    residual(p - 1, last)
                for k in (17, 20, 23, 26):
                    tree(p, k, first)

            pool.wait_ge(xn_ready[2], 1)
            pool.wait_ge(pads, PADS)
            pool.wait_ge(l1_in, L1_IN)
            load_pair(0, slice(0, 1))
            keys(0)
            low_k(0)
            pair(0, None, slice(1, 2), True)
            pair(1, slice(0, 1), slice(2, 3), False)
            with pool.Fori(1, PAIRS // 2) as i:
                for b in range(2):
                    pair(2 * i + b, bass.ds(2 * i + b - 1, 1), bass.ds(2 * i + b + 1, 1), False)
            normalise(PAIRS - 1)
            residual(PAIRS - 1, slice(PAIRS - 1, PAIRS))

            pool.wait_ge(xn_ready[3], 1)
            pool.wait_ge(mlp_in, MLP_IN)
            with pool.Fori(0, G4 // 2) as i:
                for b in range(2):
                    pool.wait_ge(M["free"], i + 1)
                    nc.gpsimd.tensor_copy(xs5[:, b, :].rearrange("p (n d) -> p n d", d=D),
                                          xn[:, bass.ds(8 * i + 4 * b, 4), :]).then_inc(M["xs"], 1)
                for b in range(2):
                    nc.gpsimd.tensor_tensor(hb[:, b, :].rearrange("p (n d) -> p n d", d=D), h[:, bass.ds(8 * i + 4 * b, 4), :],
                                            bo[:].unsqueeze(1).to_broadcast([P, 4, D]), ALU.add).then_inc(M["hb"], 1)


def kernel(**inputs):
    import concourse.bacc as bacc
    from concourse.bass_utils import run_bass_kernel_spmd

    f = {n: np.ascontiguousarray(v) for n, v in inputs.items()}
    x = f.pop("x").reshape(PAIRS, 2, 64, 64).transpose(1, 2, 0, 3).reshape(P, PAIRS, 64)
    f["x_rows"] = np.ascontiguousarray(x)
    for new, old in (("wk0_t", "L0_attn_Wk"), ("wq0_t", "L0_attn_Wq"), ("wv0_t", "L0_attn_Wv"), ("wr0_t", "L0_attn_Wr")):
        f[new] = np.ascontiguousarray(f.pop(old).T)
    f["wqv_t"] = np.ascontiguousarray(f.pop("L1_attn_wqv_w").T)
    f["fanin_t"] = np.ascontiguousarray(f.pop("L1_attn_fanin_w").T)
    f["wi_t"] = np.ascontiguousarray(f.pop("L1_ffn_Wi").T)
    f["wo_t"] = np.ascontiguousarray(f.pop("L1_ffn_Wo").T)
    f["wrb_t"] = np.concatenate([f.pop("L1_ffn_Wr").transpose(3, 0, 1, 2), f.pop("L1_ffn_br").transpose(2, 0, 1)[..., None]], 3)
    f["wsb_t"] = np.concatenate([f.pop("L1_ffn_Ws")[:, 0].transpose(2, 0, 1), f.pop("L1_ffn_bs")[:, 0].T[..., None]], 2)
    f.update(constants())
    nc = bacc.Bacc("TRN2", target_bir_lowering=False, num_devices=1)
    a = {n: nc.dram_tensor("in_" + n, v.shape, mybir.dt.from_np(v.dtype), kind="ExternalInput").ap() for n, v in f.items()}
    out = nc.dram_tensor("out", (IMGS, S, D), F32, kind="ExternalOutput").ap()
    scratch = nc.dram_tensor("token_rows", (IMGS * S, D), F32, kind="Internal").ap()
    build(nc, a, out, scratch)
    r = run_bass_kernel_spmd(nc, [{"in_" + n: v for n, v in f.items()}], core_ids=[0])
    return r.results[0]["out"]
```
